# Optimizing a Trainium2 kernel written in Bass

```python
import numpy as np
import jax
import jax.numpy as jnp

def _softmax(x, axis=-1):
    return jax.nn.softmax(x, axis=axis)

def _gelu(x):
    return jax.nn.gelu(x, approximate=True)

def _silu(x):
    return jax.nn.silu(x)

def _sigmoid(x):
    return jax.nn.sigmoid(x)

def _layernorm(x, axis=-1, eps=1e-05):
    m = jnp.mean(x, axis=axis, keepdims=True)
    v = jnp.var(x, axis=axis, keepdims=True)
    return (x - m) / jnp.sqrt(v + eps)

def _scatter_add(tgt, idx, src, axis=0):
    return tgt.at[idx].add(src)

def _segment_sum(src, seg, n):
    return jax.ops.segment_sum(src, seg, n)
kernel_name = 'mk_xattn_ffn_d1_seqx_r2_bb17bc'

def setup_inputs(seed: int=0):
    np.random.seed(seed)
    _w = jnp.asarray

    def _rec_inputs():
        import jax
        import jax.numpy as jnp
        _rk = jax.random.key(seed)
        x = -0.0003929 + 0.9999 * jax.random.normal(jax.random.fold_in(_rk, 1), (16, 1024, 512), jnp.float32)
        _lenS = 1024 - jax.random.randint(jax.random.fold_in(_rk, 7), (16,), 0, max(1, 1024 // 4) + 1, jnp.int32)
        _lenS2 = 64 - jax.random.randint(jax.random.fold_in(_rk, 8), (16,), 0, max(1, 64 // 4) + 1, jnp.int32)
        _ctx_768P = jax.random.normal(jax.random.fold_in(_rk, 11), (16, 16, 384), jnp.float32)
        _ctx_768c = jax.random.dirichlet(jax.random.fold_in(_rk, 511), 0.3 * jnp.ones((16,), jnp.float32), (16, 64))
        _ctx_768t = jnp.einsum('bsk,bkd->bsd', _ctx_768c, _ctx_768P)
        _ctx_768t = _ctx_768t * jax.lax.rsqrt(jnp.mean(jnp.square(_ctx_768t)) + 1e-12) * 0.953939
        ctx_768 = 2.09791e-05 + 1.00001 * (_ctx_768t + 0.3 * jax.random.normal(jax.random.fold_in(_rk, 611), (16, 64, 384), jnp.float32))
        return (x, ctx_768)
    x, ctx_768 = _rec_inputs()

    def _L0_xattn_setup():
        import jax, jax.numpy as jnp
        import numpy as np
        HEADS = 8
        DIM_HEAD = 64
        QUERY_DIM = 512
        CONTEXT_DIM = 384
        INNER = HEADS * DIM_HEAD
        key = jax.random.key(seed)
        ks = jax.random.split(key, 7)
        B, Sq, Skv = (4, 2048, 512)
        x = jax.random.normal(ks[0], (B, Sq, QUERY_DIM), dtype=jnp.float32)
        context = jax.random.normal(ks[1], (B, Skv, CONTEXT_DIM), dtype=jnp.float32)
        Wq = jax.random.normal(ks[2], (QUERY_DIM, INNER), dtype=jnp.float32) * QUERY_DIM ** (-0.5)
        Wk = jax.random.normal(ks[3], (CONTEXT_DIM, INNER), dtype=jnp.float32) * CONTEXT_DIM ** (-0.5)
        Wv = jax.random.normal(ks[4], (CONTEXT_DIM, INNER), dtype=jnp.float32) * CONTEXT_DIM ** (-0.5)
        Wo = jax.random.normal(ks[5], (INNER, QUERY_DIM), dtype=jnp.float32) * INNER ** (-0.5)
        bo = jax.random.normal(ks[6], (QUERY_DIM,), dtype=jnp.float32) * 0.01
        return {'x': x, 'context': context, 'Wq': Wq, 'Wk': Wk, 'Wv': Wv, 'Wo': Wo, 'bo': bo}
    _L0_xattn_all = _L0_xattn_setup()
    _L0_xattn_in = {k: v for k, v in _L0_xattn_all.items() if k in ('Wq', 'Wk', 'Wv', 'Wo', 'bo')}
    del _L0_xattn_all

    def _L0_ffn_setup():
        import jax, jax.numpy as jnp
        import numpy as np
        D = 512
        I = 256
        E = 32
        K = 4
        T = 2 * 1024
        C = 2 * T * K // E
        key = jax.random.key(seed)
        ks = jax.random.split(key, 9)
        bf = jnp.bfloat16
        std = 0.02
        x = jax.random.normal(ks[0], (2, 1024, D), dtype=jnp.float32).astype(bf)
        gate_w = (std * jax.random.normal(ks[1], (E, D), dtype=jnp.float32)).astype(bf)
        bias = jnp.zeros((E,), jnp.float32)
        W1 = (std * jax.random.normal(ks[2], (E, D, I), dtype=jnp.float32)).astype(bf)
        W3 = (std * jax.random.normal(ks[3], (E, D, I), dtype=jnp.float32)).astype(bf)
        W2 = (std * jax.random.normal(ks[4], (E, I, D), dtype=jnp.float32)).astype(bf)
        sw1 = (std * jax.random.normal(ks[5], (I, D), dtype=jnp.float32)).astype(bf)
        sw3 = (std * jax.random.normal(ks[6], (I, D), dtype=jnp.float32)).astype(bf)
        sw2 = (std * jax.random.normal(ks[7], (D, I), dtype=jnp.float32)).astype(bf)
        return {'x': x, 'gate_w': gate_w, 'bias': bias, 'W1': W1, 'W3': W3, 'W2': W2, 'sw1': sw1, 'sw3': sw3, 'sw2': sw2}
    _L0_ffn_all = _L0_ffn_setup()
    _L0_ffn_in = {k: v for k, v in _L0_ffn_all.items() if k in ('gate_w', 'bias', 'W1', 'W3', 'W2', 'sw1', 'sw3', 'sw2')}
    del _L0_ffn_all
    return {'x': x, 'ctx_768': ctx_768, 'L0_xattn_Wq': _L0_xattn_in['Wq'], 'L0_xattn_Wk': _L0_xattn_in['Wk'], 'L0_xattn_Wv': _L0_xattn_in['Wv'], 'L0_xattn_Wo': _L0_xattn_in['Wo'], 'L0_xattn_bo': _L0_xattn_in['bo'], 'L0_ffn_gate_w': _L0_ffn_in['gate_w'], 'L0_ffn_bias': _L0_ffn_in['bias'], 'L0_ffn_W1': _L0_ffn_in['W1'], 'L0_ffn_W3': _L0_ffn_in['W3'], 'L0_ffn_W2': _L0_ffn_in['W2'], 'L0_ffn_sw1': _L0_ffn_in['sw1'], 'L0_ffn_sw3': _L0_ffn_in['sw3'], 'L0_ffn_sw2': _L0_ffn_in['sw2']}

def reference(x, ctx_768, L0_xattn_Wq, L0_xattn_Wk, L0_xattn_Wv, L0_xattn_Wo, L0_xattn_bo, L0_ffn_gate_w, L0_ffn_bias, L0_ffn_W1, L0_ffn_W3, L0_ffn_W2, L0_ffn_sw1, L0_ffn_sw3, L0_ffn_sw2):
    import jax
    import jax.numpy as jnp

    def _L0_xattn_ref(x, context, Wq, Wk, Wv, Wo, bo):
        import jax, jax.numpy as jnp
        import numpy as np
        HEADS = 8
        DIM_HEAD = 64
        QUERY_DIM = 512
        CONTEXT_DIM = 384
        INNER = HEADS * DIM_HEAD
        B, Sq, _ = x.shape
        h, d = (HEADS, DIM_HEAD)
        scale = d ** (-0.5)
        q = (x @ Wq).reshape(B, Sq, h, d).transpose(0, 2, 1, 3)
        k = (context @ Wk).reshape(B, -1, h, d).transpose(0, 2, 1, 3)
        v = (context @ Wv).reshape(B, -1, h, d).transpose(0, 2, 1, 3)
        scores = jnp.einsum('bhid,bhjd->bhij', q, k) * scale
        attn = jax.nn.softmax(scores, axis=-1)
        out = jnp.einsum('bhij,bhjd->bhid', attn, v)
        out = out.transpose(0, 2, 1, 3).reshape(B, Sq, h * d)
        return out @ Wo + bo

    def _L0_ffn_ref(x, gate_w, bias, W1, W3, W2, sw1, sw3, sw2):
        import jax, jax.numpy as jnp
        import numpy as np
        D = 512
        I = 256
        E = 32
        K = 4
        T = 2 * 1024
        C = 2 * T * K // E
        X = x.reshape(-1, D)
        logits = (X @ gate_w.T).astype(jnp.float32)
        scores = jax.nn.sigmoid(logits)
        _, idx = jax.lax.top_k(scores + bias[None, :], K)
        w = jnp.take_along_axis(scores, idx, axis=-1)
        w = w / jnp.clip(jnp.sum(w, axis=-1, keepdims=True), 1e-12, None)
        w = w.astype(x.dtype)
        eid = idx.reshape(-1)
        onehot = (eid[:, None] == jnp.arange(E)[None, :]).astype(jnp.int32)
        pos = jnp.take_along_axis(jnp.cumsum(onehot, axis=0) - 1, eid[:, None], axis=1)[:, 0]
        valid = pos < C
        posc = jnp.minimum(pos, C - 1)
        Xrep = jnp.repeat(X, K, axis=0)
        xe = jnp.zeros((E, C, D), x.dtype).at[eid, posc].add(jnp.where(valid[:, None], Xrep, jnp.zeros((), x.dtype)))
        h = jax.nn.silu(jnp.einsum('ecd,edi->eci', xe, W1)) * jnp.einsum('ecd,edi->eci', xe, W3)
        ye = jnp.einsum('eci,eid->ecd', h, W2)
        gflat = jnp.where(valid, w.reshape(-1), jnp.zeros((), x.dtype))
        yrows = ye[eid, posc] * gflat[:, None]
        out = yrows.reshape(-1, K, D).sum(axis=1)
        out = out + jax.nn.silu(X @ sw1.T) * (X @ sw3.T) @ sw2.T
        return out.reshape(x.shape)
    x = x + _L0_xattn_ref(_layernorm(x, axis=-1), ctx_768, L0_xattn_Wq, L0_xattn_Wk, L0_xattn_Wv, L0_xattn_Wo, L0_xattn_bo)
    x = x + _L0_ffn_ref(_layernorm(x, axis=-1), L0_ffn_gate_w, L0_ffn_bias, L0_ffn_W1, L0_ffn_W3, L0_ffn_W2, L0_ffn_sw1, L0_ffn_sw3, L0_ffn_sw2)
    return x

_drawn_inputs = setup_inputs


def setup_inputs(seed=0):
    import zlib

    import numpy as np

    out = dict(_drawn_inputs(seed))
    spreads = {'L0_ffn_bias': (0.0, 0.8)}
    factors = {'L0_xattn_bo': 6.285,
     'L0_ffn_gate_w': 8.0,
     'L0_ffn_W1': 8.0,
     'L0_ffn_W3': 8.0,
     'L0_ffn_W2': 8.0,
     'L0_ffn_sw1': 6.742,
     'L0_ffn_sw3': 6.179,
     'L0_ffn_sw2': 6.186}
    for name, (base, spread) in spreads.items():
        noise = np.random.default_rng([zlib.crc32(name.encode()), seed]).standard_normal(out[name].shape)
        drawn = base * np.exp(spread * noise) if base else spread * noise
        out[name] = jnp.asarray(drawn.astype(out[name].dtype))
    for name, factor in factors.items():
        out[name] = (out[name] * factor).astype(out[name].dtype)
    return out
```

```python
from contextlib import ExitStack

import concourse.bass as bass
from concourse import mybir

F32 = mybir.dt.float32
F32R = mybir.dt.float32r
F16 = mybir.dt.float16
BF16 = mybir.dt.bfloat16
I32 = mybir.dt.int32
U32 = mybir.dt.uint32
ALU = mybir.AluOpType
ACT = mybir.ActivationFunctionType
AX = mybir.AxisListType

P = 128
B, S, D = 16, 1024, 512
SKV, DC = 64, 384
H, DH = 8, 64
KD, KC = D // P, DC // P
PAIRS = H // 2
E, TOP, CAP, I = 32, 4, 512, 256
TOKENS = B * S
TILES = TOKENS // P
GROUPS = TILES // 4
TPB = S // P
SLOTS = E * CAP
KI = I // P
ROW = D + E
PAD = CAP
EPS = 1e-5
SKIP = float(1 << 20)
MAGIC = 1597463007.0

BODY = 16
LAST_LAG = 21
STEPS = TILES - 4 + LAST_LAG + 1


class Index:

    def __init__(self, it, m, c):
        self.it, self.m, self.c = it, m, c

    def __add__(self, n):
        return Index(self.it, self.m, self.c + n)

    def __sub__(self, n):
        return self + -n

    def __mul__(self, n):
        return Index(self.it, self.m * n, self.c * n)

    def __floordiv__(self, n):
        assert self.m % n == 0
        return Index(self.it, self.m // n, self.c // n)

    def __mod__(self, n):
        assert self.m % n == 0
        return self.c % n

    def value(self):
        return self.m * self.it + self.c

    def count(self):
        v = self.value()
        return max(v, 0) if isinstance(v, int) else v


class Step:

    def __init__(self, it, s):
        self.it, self.s = it, s

    def at(self, lag, per=1, total=TILES):
        n = Index(self.it, BODY, self.s - lag)
        if n.c % per:
            return None
        n = n // per
        if isinstance(self.it, int) and not 0 <= n.value() < total:
            return None
        return n

    def group(self, lag):
        return self.at(lag, 4, GROUPS)

    def batch(self, lag):
        return self.at(lag, TPB, B)


def steps(eng, step):
    for n in range(2 * BODY):
        step(Step(n // BODY, n % BODY))
    with eng.Fori(2, TILES // BODY) as it:
        for s in range(BODY):
            step(Step(it, s))
    for n in range(TILES, STEPS):
        step(Step(n // BODY, n % BODY))


def build(nc, x, xT, ctxT, wqT, wk, wv, wo, bo, gateT, bias, w1, w3, w2, sw1T, sw3T, sw2T, out):
    x2aug = nc.dram_tensor("x2aug", (TOKENS + PAD, ROW), F32, kind="Internal").ap()
    table = nc.dram_tensor("slot_table", (SLOTS, 1), I32, kind="Internal").ap()
    set_up_and_tokens(nc, x, xT, ctxT, wqT, wk, wv, wo, bo, gateT, bias, sw1T, sw3T, sw2T, out, x2aug, table)
    experts(nc, w1, w3, w2, out, x2aug, table)


def set_up_and_tokens(nc, x, xT, ctxT, wqT, wk, wv, wo, bo, gateT, bias, sw1T, sw3T, sw2T, out, x2aug, table):
    stack = ExitStack()
    with stack:
        def sb(name, shape, dt):
            return stack.enter_context(nc.sbuf_tensor(name, shape, dt))

        def pb(name):
            return stack.enter_context(nc.psum_tensor(name, [P, 512], F32))

        def sem(name):
            return stack.enter_context(nc.semaphore(name))

        wqc = sb("wqc", [P, PAIRS, D], F32)
        wo_sb = sb("wo_sb", [P, PAIRS, D], F32)
        wk_sb = sb("wk_sb", [P, KC, H * DH], F32)
        wv_sb = sb("wv_sb", [P, KC, H * DH], F32)
        bo_hi = sb("bo_hi", [1, D], F32R)
        bo_lo = sb("bo_lo", [1, D], F32R)
        head0 = sb("head0", [1, P], F32R)
        gate_sb = sb("gate_sb", [P, KD, E], BF16)
        bias_sb = sb("bias_sb", [P, E], F32)
        up_sb = sb("up_sb", [P, KD, 2 * I], BF16)
        down_sb = sb("down_sb", [P, KI, D], F32R)
        ident = sb("ident", [P, P], F32)
        earlier = sb("earlier", [P, P], BF16)
        ones = sb("ones", [P, P], BF16)
        iota_e = sb("iota_e", [P, E], F32)
        tok = sb("tok", [P, 16], I32)
        xr = sb("xr", [P, 16, D], F32)
        xt = sb("xt", [P, 2, KD, P], F32)
        xt_h = sb("xt_h", [P, 2, KD, P], F32R)
        xt_l = sb("xt_l", [P, 2, KD, P], F32R)
        a_h = sb("a_h", [P, 2, KD, D], F32R)
        a_l = sb("a_l", [P, 2, KD, D], F32R)
        m_h = sb("m_h", [P, 2, PAIRS, D], F32R)
        m_l = sb("m_l", [P, 2, PAIRS, D], F32R)
        prep_full = sb("prep_full", [P, D], F32)
        ctx_sb = sb("ctx_sb", [P, KC, SKV], F32)
        kbd = sb("kbd", [P, PAIRS, P], F32)
        vbd = sb("vbd", [P, PAIRS, P], F32)
        below = sb("below", [P, H, SKV], F32)
        prob = sb("prob", [P, 2, H, SKV], F32)
        pt_h = sb("pt_h", [P, PAIRS, P], F32R)
        pt_l = sb("pt_l", [P, PAIRS, P], F32R)
        top_s = sb("top_s", [P, H], F32)
        sums = sb("sums", [P, H], F32)
        rsum = sb("rsum", [P, H], F32)
        x2 = sb("x2", [P, 2, D], F32)
        x2t_h = sb("x2t_h", [P, 2, KD, 4 * P], F16)
        x2t_l = sb("x2t_l", [P, 2, KD, 4 * P], F16)
        th = sb("th", [P, 4 * P], F32)
        hid = sb("hid", [P, 4 * P], F32)
        ht_h = sb("ht_h", [P, KI, 4 * P], F32R)
        ht_l = sb("ht_l", [P, KI, 4 * P], F32R)
        st1 = sb("st1", [P, 4, 6], F32)
        mv1 = sb("mv1", [P, 4, 2], F32)
        nt1 = sb("nt1", [P, 3, 4], F32)
        rs1 = sb("rs1", [P, 2, 4], F32)
        st2 = sb("st2", [P, 6], F32)
        mv2 = sb("mv2", [P, 2], F32)
        nt2 = sb("nt2", [P, 3], F32)
        rs2 = sb("rs2", [P, 1], F32)
        nb2 = sb("nb2", [P, 1], F32)
        lexp = sb("lexp", [P, 4, E], F32)
        score = sb("score", [P, 4, E], F32)
        biased = sb("biased", [P, 4, E], F32)
        best = sb("best", [P, 4, 8], F32)
        best_at = sb("best_at", [P, 4, 8], U32)
        best_f = sb("best_f", [P, 4, TOP], F32)
        pick = sb("pick", [P, 4 * TOP, E], F32)
        member = sb("member", [P, 4, E], BF16)
        before = sb("before", [P, E], BF16)
        gsum = sb("gsum", [P, E], F32)
        wm = sb("wm", [P, 4, E], F32)
        wsum = sb("wsum", [P, 4], F32)
        wr = sb("wr", [P, 4], F32)
        wfull = sb("wfull", [P, 2, 4, E], F32)
        pos_k = sb("pos_k", [P, 4 * TOP], F32)
        over = sb("over", [P, 4 * TOP], F32)
        slot_f = sb("slot_f", [P, 4 * TOP], F32)
        slot = sb("slot", [P, 2, 4 * TOP], I32)

        S_ps, TP_ps, O_ps, TX_ps = pb("S_ps"), pb("TP_ps"), pb("O_ps"), pb("TX_ps")
        G_ps, U_ps, PREP_ps, R_ps = pb("G_ps"), pb("U_ps"), pb("PREP_ps"), pb("R_ps")
        logit_ps = R_ps[:, 0:4 * E].rearrange("p (i e) -> p i e", i=4)
        rank_ps = R_ps[:, 4 * E:8 * E].rearrange("p (i e) -> p i e", i=4)

        raw_load, small_load, fill_store = sem("raw_load"), sem("small_load"), sem("fill_store")
        set_p, set_v, set_a = sem("set_p"), sem("set_v"), sem("set_a")
        rawstack = ExitStack()
        with rawstack:
            zrow = xr[:, 8:10, :].rearrange("p a d -> p (a d)")[:, 0:ROW]
            fill = xr[:, 10, 0:SLOTS // P].bitcast(I32)
            down_raw = xr[:, 11, :].bitcast(BF16).rearrange("p (c d) -> p c d", c=KI)
            bo_raw = xr[0:1, 12, :]
            mean_q = xr[:, 13, 0:PAIRS]
            with nc.Block() as block:
                @block.sync
                def _(sp):
                    sp.dma_start(wqc[:, :, :], wqT.rearrange("(c p) d -> p c d", p=P)).then_inc(raw_load, 16)
                    sp.dma_start(down_raw, sw2T.rearrange("(c p) d -> p c d", p=P)).then_inc(small_load, 16)
                    sp.dma_start(bo_raw, bo.rearrange("(a d) -> a d", a=1)).then_inc(small_load, 16)
                    sp.dma_start(wk_sb[:, :, :], wk.rearrange("(c p) d -> p c d", p=P)).then_inc(raw_load, 16)
                    sp.dma_start(wv_sb[:, :, :], wv.rearrange("(c p) d -> p c d", p=P)).then_inc(raw_load, 16)
                    sp.dma_start(wo_sb[:, :, :], wo.rearrange("(c p) d -> p c d", p=P)).then_inc(raw_load, 16)
                    sp.dma_start(up_sb[:, :, 0:I], sw1T.rearrange("(c p) i -> p c i", p=P)).then_inc(raw_load, 16)
                    sp.dma_start(up_sb[:, :, I:2 * I], sw3T.rearrange("(c p) i -> p c i", p=P)).then_inc(raw_load, 16)
                    sp.dma_start(gate_sb[:, :, :], gateT.rearrange("(c p) e -> p c e", p=P)).then_inc(raw_load, 16)
                    sp.dma_start(bias_sb[:, :], bias).then_inc(raw_load, 16)
                    sp.wait_ge(set_p, 2)
                    for r in range(TOKENS, TOKENS + PAD, P):
                        sp.dma_start(x2aug[r:r + P, :], zrow).then_inc(fill_store, 16)
                        sp.dma_start(out[r:r + P, :], zrow[:, 0:D]).then_inc(fill_store, 16)
                    sp.dma_start(table.rearrange("(e p c) o -> p e (c o)", e=E, p=P),
                                 fill.rearrange("p (e c) -> p e c", e=E)).then_inc(fill_store, 16)
                    sp.wait_ge(raw_load, 8 * 16)
                    sp.wait_ge(fill_store, (2 * PAD // P + 1) * 16)

                @block.gpsimd
                def _(pool):
                    pool.memset(zrow, 0.0).then_inc(set_p, 1)
                    pool.iota(fill.rearrange("p (e c) -> p e c", e=E), [[0, E], [1, CAP // P]], base=TOKENS,
                              channel_multiplier=CAP // P).then_inc(set_p, 1)
                    pool.iota(tok[:, :], [[P, 16]], base=0, channel_multiplier=1).then_inc(set_p, 1)
                    pool.iota(iota_e[:, :], [[1, E]], base=0, channel_multiplier=0, allow_small_or_imprecise_dtypes=True).then_inc(set_p, 1)
                    pool.memset(ident[:, :], 0.0).then_inc(set_p, 1)
                    pool.memset(earlier[:, :], 0.0).then_inc(set_p, 1)
                    pool.memset(ones[:, :], 1.0).then_inc(set_p, 1)
                    pool.memset(kbd[:, :, :], 0.0).then_inc(set_p, 1)
                    pool.memset(vbd[:, :, :], 0.0).then_inc(set_p, 1)
                    pool.memset(before[:, :], 0.0).then_inc(set_p, 1)
                    pool.wait_ge(set_p, 6)
                    pool.affine_select(out=ident[:, :], in_=ident[:, :], compare_op=ALU.not_equal, fill=1.0,
                                       base=0, pattern=[[-1, P]], channel_multiplier=1).then_inc(set_p, 1)
                    pool.affine_select(out=earlier[:, :], in_=earlier[:, :], compare_op=ALU.is_ge, fill=1.0,
                                       base=0, pattern=[[-1, P]], channel_multiplier=1).then_inc(set_p, 1)

                @block.vector
                def _(dve):
                    dve.memset(head0[:, :].bitcast(F32), 0.0).then_inc(set_v, 1)
                    dve.wait_ge(set_v, 1)
                    dve.memset(head0[:, 0:DH].bitcast(F32), 1.0).then_inc(set_v, 1)
                    dve.wait_ge(raw_load, 8 * 16)
                    dve.tensor_reduce(mean_q, wqc[:, :, :], AX.X, ALU.add).then_inc(set_v, 1)
                    dve.wait_ge(set_v, 3)
                    dve.tensor_scalar(mean_q, mean_q, 1.0 / D, None, ALU.mult).then_inc(set_v, 1)
                    dve.wait_ge(set_v, 4)
                    for c in range(PAIRS):
                        dve.tensor_scalar(wqc[:, c, :], wqc[:, c, :], mean_q[:, c:c + 1], None, ALU.subtract)
                    dve.wait_ge(set_a, 1)
                    dve.tensor_tensor(bo_lo[:, :], bo_raw, bo_hi[:, :].bitcast(F32), ALU.subtract)

                @block.scalar
                def _(act):
                    act.wait_ge(small_load, 2 * 16)
                    act.activation(bo_hi[:, :], bo_raw, ACT.Copy).then_inc(set_a, 1)
                    act.activation(down_sb[:, :, :], down_raw, ACT.Copy)

        x_loaded = [sem(f"x_loaded{g}") for g in range(4)]
        xt_loaded = [sem(f"xt_loaded{t}") for t in range(2)]
        ctx_loaded = sem("ctx_loaded")
        out_stored = [sem(f"out_stored{g}") for g in range(4)]
        x2_stored = [sem(f"x2_stored{t}") for t in range(2)]
        w_stored = [sem(f"w_stored{g}") for g in range(2)]
        scattered = [sem(f"scattered{g}") for g in range(4)]
        xt_hi, xt_lo = sem("xt_hi"), sem("xt_lo")
        scores_done, probs_t_done, o_done = sem("scores_done"), sem("probs_t_done"), sem("o_done")
        x2_t_done, logits_done = sem("x2_t_done"), sem("logits_done")
        max_done, below_done, sum_done, rsum_done = sem("max_done"), sem("below_done"), sem("sum_done"), sem("rsum_done")
        exp_done, pt_hi, x2_done, x2t_hi = sem("exp_done"), sem("pt_hi"), sem("x2_done"), sem("x2t_hi")
        prob_done = sem("prob_done")
        pt_lo, x1_done, x2t_lo = sem("pt_lo"), sem("x1_done"), sem("x2t_lo")
        bn1, agg1, ln1 = sem("bn1"), sem("agg1"), sem("ln1")
        bn2, agg2, ln2 = sem("bn2"), sem("agg2"), sem("ln2")
        prep_done, prep_hi, prep_lo = sem("prep_done"), sem("prep_hi"), sem("prep_lo")
        g_done, u_done = sem("g_done"), sem("u_done")
        g_free, u_free = sem("g_free"), sem("u_free")
        th_done, ht_hi, ht_lo = sem("th_done"), sem("ht_hi"), sem("ht_lo")
        lexp_done, rank_done = sem("lexp_done"), sem("rank_done")
        route_a, route_b = sem("route_a"), sem("route_b")
        joined = sem("joined")
        w_ready, slots_ready = sem("w_ready"), sem("slots_ready")
        passed = sem("passed")
        tok_ready = sem("tok_ready")
        LN1_OPS, LN2_OPS = 12, 13
        ROUTE_A, ROUTE_B = 14, 9

        x_groups = x[0:TOKENS, :].rearrange("(g i p) d -> g p i d", i=4, p=P)
        out_groups = out[0:TOKENS, :].rearrange("(g i p) d -> g p i d", i=4, p=P)
        x2_tiles = x2aug[0:TOKENS, :].rearrange("(t p) r -> t p r", p=P)
        w_groups = x2aug[0:TOKENS, :].rearrange("(g i p) r -> g p i r", i=4, p=P)
        ctx_batches = ctxT.rearrange("b (c p) j -> b p c j", p=P)

        with nc.Block() as block:
            @block.sync
            def _(sp):
                def step(k):
                    b = k.batch(0)
                    if b is not None:
                        sp.wait_ge(prep_done, (b * 9 - 8).count())
                        sp.dma_start(ctx_sb[:, :, :], ctx_batches[b.value()]).then_inc(ctx_loaded, 16)
                    g = k.group(18)
                    if g is not None:
                        sp.wait_ge(g_free, (g * 4 + 4).count())
                        sp.wait_ge(u_free, (g * 4 + 4).count())
                        r = g % 4
                        sp.dma_start(out_groups[g.value()], xr[:, 4 * r:4 * r + 4, :]).then_inc(out_stored[r], 16)
                    g = k.group(3)
                    if g is not None:
                        r = g % 4
                        sp.wait_ge(out_stored[r], ((g // 4) * 16).count())
                        sp.dma_start(xr[:, 4 * r:4 * r + 4, :], x_groups[g.value()]).then_inc(x_loaded[r], 16)
                    t = k.at(5)
                    if t is not None:
                        sp.wait_ge(xt_lo, (t - 1).count())
                        sp.wait_ge(xt_hi, (t - 1).count())
                        sp.dma_start(xt[:, t % 2], xT[t.value()]).then_inc(xt_loaded[t % 2], 16)
                    g = k.group(17)
                    if g is not None:
                        sp.wait_ge(w_ready, (g + 1).count())
                        sp.dma_start(w_groups[g.value()][:, :, D:ROW], wfull[:, g % 2]).then_inc(w_stored[g % 2], 16)
                    t = k.at(10)
                    if t is not None:
                        sp.wait_ge(x2_done, (t + 1).count())
                        sp.dma_start(x2_tiles[t.value()][:, 0:D], x2[:, t % 2, :]).then_inc(x2_stored[t % 2], 16)

                steps(sp, step)
                for r in range(4):
                    sp.wait_ge(out_stored[r], GROUPS // 4 * 16)
                for r in range(2):
                    sp.wait_ge(x2_stored[r], TILES // 2 * 16)
                    sp.wait_ge(w_stored[r], GROUPS // 2 * 16)

            @block.tensor
            def _(pe):
                def prep_chunk(b, j):
                    pe.wait_ge(prep_hi, (b * 9 + j + 1).count())
                    if j < KD:
                        for p in range(PAIRS):
                            last = pe.matmul(PREP_ps[:, p * P:(p + 1) * P], wqc[:, p, j * P:(j + 1) * P],
                                             kbd[:, p, :], start=True, stop=True)
                    else:
                        p = j - KD
                        last = pe.matmul(PREP_ps[:, :], vbd[:, p, :], wo_sb[:, p, :], start=True, stop=(p > 0))
                        if p == 0:
                            pe.matmul(PREP_ps[:, :], head0[:, :], bo_hi[:, :], start=False, stop=False)
                            last = pe.matmul(PREP_ps[:, :], head0[:, :], bo_lo[:, :], start=False, stop=True)
                    last.then_inc(prep_done, 1)

                def up_half(bank, w0, g, c):
                    n = 0
                    for kc in range(KD):
                        for part in (x2t_h, x2t_l):
                            last = pe.matmul(bank[:, :], up_sb[:, kc, w0 + c * P:w0 + (c + 1) * P],
                                             part[:, g % 2, kc, :], start=(n == 0), stop=(n == 2 * KD - 1))
                            n += 1
                    return last

                def down_tile(bank, i):
                    n = 0
                    for c in range(KI):
                        for part in (ht_h, ht_l):
                            last = pe.matmul(bank[:, :], part[:, c, i * P:(i + 1) * P], down_sb[:, c, :],
                                             start=(n == 0), stop=(n == 2 * KI - 1))
                            n += 1
                    return last

                def step(k):
                    t = k.at(8)
                    if t is not None:
                        b = t // TPB
                        if t % TPB == 0:
                            pe.wait_ge(prep_hi, (b * 9 + 5).count())
                            pe.wait_ge(prep_lo, (b * 8 + 4).count())
                        pe.wait_ge(xt_hi, (t + 1).count())
                        pe.wait_ge(xt_lo, (t + 1).count())
                        pe.wait_ge(below_done, t.count())
                        n = 0
                        for kc in range(KD):
                            for left, right in ((xt_h, a_h), (xt_h, a_l), (xt_l, a_h)):
                                last = pe.matmul(S_ps[:, :], left[:, t % 2, kc, :], right[:, b % 2, kc, :],
                                                 start=(n == 0), stop=(n == 3 * KD - 1))
                                n += 1
                        last.then_inc(scores_done, 1)
                    t = k.at(11)
                    if t is not None:
                        pe.wait_ge(x2_done, (t + 1).count())
                        pe.wait_ge(x2t_hi, t.count())
                        pe.wait_ge(x2t_lo, t.count())
                        for kc in range(KD):
                            last = pe.transpose(TX_ps[:, kc * P:(kc + 1) * P], x2[:, t % 2, kc * P:(kc + 1) * P],
                                                ident[:, :])
                        last.then_inc(x2_t_done, 1)
                    g = k.group(16)
                    if g is not None:
                        pe.wait_ge(route_a, (g * ROUTE_A + ROUTE_A).count())
                        pe.wait_ge(route_b, (g * ROUTE_B).count())
                        pe.matmul(rank_ps, earlier[:, :], member[:, :, :], start=True, stop=False)
                        for i in range(3):
                            pe.matmul(rank_ps[:, i + 1:4, :], ones[:, :],
                                      member[:, i:i + 1, :].to_broadcast([P, 3 - i, E]), start=False, stop=False)
                        pe.matmul(rank_ps, ones[:, :], before[:, :].unsqueeze(1).to_broadcast([P, 4, E]),
                                  start=False, stop=True).then_inc(rank_done, 1)
                    t = k.at(9)
                    if t is not None:
                        pe.wait_ge(prob_done, (t + 1).count())
                        pe.wait_ge(pt_hi, t.count())
                        pe.wait_ge(pt_lo, t.count())
                        for p in range(PAIRS):
                            last = pe.transpose(TP_ps[:, p * P:(p + 1) * P],
                                                prob[:, t % 2, 2 * p:2 * p + 2, :].rearrange("p h j -> p (h j)"),
                                                ident[:, :])
                        last.then_inc(probs_t_done, 1)
                    s8 = k.s % TPB
                    if s8:
                        b = k.batch(s8)
                        if b is not None:
                            prep_chunk(b, s8 - 1)
                    else:
                        b = k.batch(TPB)
                        if b is not None:
                            prep_chunk(b, TPB - 1)
                    t = k.at(11)
                    if t is not None:
                        g, i = t // 4, t % 4
                        pe.wait_ge(x2t_hi, (t + 1).count())
                        pe.wait_ge(x2t_lo, (t + 1).count())
                        if i == 0:
                            pe.wait_ge(lexp_done, g.count())
                        n = 0
                        for kc in range(KD):
                            for part in (x2t_h, x2t_l):
                                last = pe.matmul(logit_ps[:, i, :], part[:, g % 2, kc, i * P:(i + 1) * P],
                                                 gate_sb[:, kc, :], start=(n == 0), stop=(n == 2 * KD - 1))
                                n += 1
                        last.then_inc(logits_done, 1)
                    for c in range(2):
                        g = k.group(14 + c)
                        if g is not None:
                            pe.wait_ge(x2t_hi, (g * 4 + 4).count())
                            pe.wait_ge(x2t_lo, (g * 4 + 4).count())
                            pe.wait_ge(g_free, (g * 4 + c).count())
                            up_half(G_ps, 0, g, c).then_inc(g_done, 1)
                            pe.wait_ge(u_free, (g * 4 + c).count())
                            up_half(U_ps, I, g, c).then_inc(u_done, 1)
                    for j in range(2):
                        g = k.group(16 + j)
                        if g is not None:
                            pe.wait_ge(ht_hi, (g * 2 + 2).count())
                            pe.wait_ge(ht_lo, (g * 2 + 2).count())
                            pe.wait_ge(g_free, (g * 4 + 2 + j).count())
                            down_tile(G_ps, 2 * j).then_inc(g_done, 1)
                            pe.wait_ge(u_free, (g * 4 + 2 + j).count())
                            down_tile(U_ps, 2 * j + 1).then_inc(u_done, 1)
                    t = k.at(9)
                    if t is not None:
                        b = t // TPB
                        if t % TPB == 0:
                            pe.wait_ge(prep_hi, (b * 9 + 9).count())
                            pe.wait_ge(prep_lo, (b * 8 + 8).count())
                        pe.wait_ge(pt_hi, (t + 1).count())
                        pe.wait_ge(pt_lo, (t + 1).count())
                        pe.wait_ge(x1_done, t.count())
                        n = 0
                        for p in range(PAIRS):
                            for left, right in ((pt_h, m_h), (pt_h, m_l), (pt_l, m_h)):
                                last = pe.matmul(O_ps[:, :], left[:, p, :], right[:, b % 2, p, :],
                                                 start=(n == 0), stop=(n == 3 * PAIRS - 1))
                                n += 1
                        last.then_inc(o_done, 1)
                    b = k.batch(0)
                    if b is not None:
                        pe.wait_ge(ctx_loaded, (b * 16 + 16).count())
                        pe.wait_ge(prep_hi, (b * 9).count())
                        for n, w in enumerate((wk_sb, wv_sb)):
                            for p in range(PAIRS):
                                col = n * PAIRS * SKV + p * SKV
                                for kc in range(KC):
                                    last = pe.matmul(PREP_ps[:, col:col + SKV], w[:, kc, p * P:(p + 1) * P],
                                                     ctx_sb[:, kc, :], start=(kc == 0), stop=(kc == KC - 1))
                        last.then_inc(prep_done, 1)

                steps(pe, step)

            @block.scalar
            def _(act):
                def step(k):
                    b = k.batch(1)
                    if b is not None:
                        act.wait_ge(prep_done, (b * 9 + 1).count())
                        kv = PREP_ps[:, :].rearrange("p (n q j) -> p n q j", n=2, q=PAIRS)
                        for n, (dst, scale) in enumerate(((kbd, DH ** -0.5), (vbd, 1.0))):
                            for h in range(2):
                                r = slice(h * DH, (h + 1) * DH)
                                last = act.activation(dst[r, :, h * SKV:(h + 1) * SKV], kv[r, n], ACT.Copy, scale=scale)
                        last.then_inc(prep_hi, 1)
                    g = k.group(15)
                    if g is not None:
                        act.wait_ge(logits_done, (g * 4 + 4).count())
                        act.wait_ge(route_a, (g * ROUTE_A).count())
                        act.activation(lexp[:, :, :], logit_ps, ACT.Exp, scale=-1.0).then_inc(lexp_done, 1)
                    t = k.at(11)
                    if t is not None:
                        g, i = t // 4, t % 4
                        act.wait_ge(x2_t_done, (t + 1).count())
                        act.wait_ge(u_done, (g * 4 - 6).count())
                        act.activation(x2t_h[:, g % 2, :, i * P:(i + 1) * P],
                                       TX_ps[:, :].rearrange("p (c t) -> p c t", c=KD), ACT.Copy).then_inc(x2t_hi, 1)
                    t = k.at(9)
                    if t is not None:
                        act.wait_ge(probs_t_done, (t + 1).count())
                        act.wait_ge(o_done, t.count())
                        act.activation(pt_h[:, :, :].rearrange("p a b -> p (a b)"), TP_ps[:, :], ACT.Copy).then_inc(pt_hi, 1)
                    t = k.at(8)
                    if t is not None:
                        g, i = t // 4, t % 4
                        act.wait_ge(below_done, (t + 1).count())
                        act.wait_ge(ln1, ((g + 1) * LN1_OPS).count())
                        act.wait_ge(probs_t_done, (t - 1).count())
                        act.activation(prob[:, t % 2, :, :], below[:, :, :], ACT.Exp,
                                       scale=rs1[:, g % 2, i:i + 1]).then_inc(exp_done, 1)
                    s8 = k.s % TPB
                    b, j = (k.batch(s8), s8 - 1) if s8 else (k.batch(TPB), TPB - 1)
                    if b is not None:
                        act.wait_ge(prep_done, (b * 9 + j + 2).count())
                        act.wait_ge(prep_lo, (b * 8 + j).count())
                        act.activation(prep_full[:, :], PREP_ps[:, :], ACT.Copy)
                        if j < KD:
                            act.wait_ge(scores_done, (b * TPB - TPB).count())
                            dst = a_h[:, b % 2, j, :]
                        else:
                            act.wait_ge(o_done, (b * TPB - TPB).count())
                            dst = m_h[:, b % 2, j - KD, :]
                        act.activation(dst, PREP_ps[:, :], ACT.Copy).then_inc(prep_hi, 1)
                    for c in range(2):
                        g = k.group(14 + c)
                        if g is not None:
                            act.wait_ge(g_done, (g * 4 + c + 1).count())
                            act.wait_ge(u_free, (g * 4 + c).count())
                            act.activation(th[:, :], G_ps[:, :], ACT.Tanh, scale=0.5).then_inc(th_done, 1)
                    t = k.at(7)
                    if t is not None:
                        act.wait_ge(xt_loaded[t % 2], ((t // 2) * 16 + 16).count())
                        act.wait_ge(scores_done, (t - 1).count())
                        act.activation(xt_h[:, t % 2, :, :], xt[:, t % 2, :, :], ACT.Copy).then_inc(xt_hi, 1)
                    t = k.at(10)
                    if t is not None:
                        act.wait_ge(ln2, ((t + 1) * LN2_OPS).count())
                        act.wait_ge(x2_t_done, (t - 1).count())
                        act.wait_ge(x2_stored[t % 2], ((t // 2) * 16).count())
                        act.activation(x2[:, t % 2, :], xr[:, t % 16, :], ACT.Identity, bias=nb2[:, 0:1],
                                       scale=rs2[:, 0:1]).then_inc(x2_done, 1)
                    for c in range(2):
                        g = k.group(14 + c)
                        if g is not None:
                            act.wait_ge(u_free, (g * 4 + c + 1).count())
                            act.wait_ge(u_done, (g * 4).count())
                            act.activation(ht_h[:, c, :], hid[:, :], ACT.Copy).then_inc(ht_hi, 1)

                steps(act, step)

            @block.gpsimd
            def _(pool):
                def step(k):
                    s8 = (k.s - 1) % TPB
                    b, j = (k.batch(s8 + 1), s8 - 1) if s8 else (k.batch(TPB + 1), TPB - 1)
                    if b is not None:
                        pool.wait_ge(prep_hi, (b * 9 + j + 2).count())
                        hi, lo = (a_h, a_l) if j < KD else (m_h, m_l)
                        pool.tensor_tensor(lo[:, b % 2, j % KD, :], prep_full[:, :], hi[:, b % 2, j % KD, :].bitcast(F32),
                                           ALU.subtract).then_inc(prep_lo, 1)
                    t = k.at(7)
                    if t is not None:
                        pool.wait_ge(xt_hi, (t + 1).count())
                        pool.tensor_tensor(xt_l[:, t % 2, :, :], xt[:, t % 2, :, :], xt_h[:, t % 2, :, :].bitcast(F32),
                                           ALU.subtract).then_inc(xt_lo, 1)
                    t = k.at(8)
                    if t is not None:
                        pool.wait_ge(rsum_done, (t + 1).count())
                        pool.tensor_tensor(prob[:, t % 2, :, :], prob[:, t % 2, :, :],
                                           rsum[:, :].unsqueeze(2).to_broadcast([P, H, SKV]), ALU.mult).then_inc(prob_done, 1)
                    for c in range(2):
                        g = k.group(14 + c)
                        if g is not None:
                            pool.wait_ge(ht_hi, (g * 2 + c + 1).count())
                            pool.tensor_tensor(ht_l[:, c, :], hid[:, :], ht_h[:, c, :].bitcast(F32),
                                               ALU.subtract).then_inc(ht_lo, 1)
                    for i in range(4):
                        g = k.group(18 + i)
                        if g is None:
                            continue
                        r = g % 4
                        again = not (isinstance(g.value(), int) and g.value() < 4)
                        if i == 0:
                            pool.wait_ge(slots_ready, (g + 1).count())
                            pool.sem_inc(passed, 1)
                            if again:
                                pool.wait_ge(scattered[r], ((g // 4) * 256).count())
                                pool.sem_inc(passed, 1)
                                pool.tensor_scalar(tok[:, 4 * r:4 * r + 4], tok[:, 4 * r:4 * r + 4], float(BODY * P), None,
                                                   ALU.add).then_inc(tok_ready, 1)
                                pool.wait_ge(tok_ready, (g - 3).count())
                                pool.sem_inc(passed, 1)
                        for q in range(TOP):
                            pool.indirect_dma_start(
                                table, bass.IndirectOffsetOnAxis(ap=slot[:, g % 2, i * TOP + q:i * TOP + q + 1], axis=0),
                                tok[:, 4 * r + i:4 * r + i + 1], None, bounds_check=SLOTS - 1,
                                oob_is_err=False).then_inc(scattered[r], 16)

                steps(pool, step)
                for r in range(4):
                    pool.wait_ge(scattered[r], GROUPS // 4 * 256)

            @block.vector
            def _(dve):
                def inv_std(sem_, base, var, v, a, y):
                    n = [0]

                    def link(ins):
                        n[0] += 1
                        ins.then_inc(sem_, 1)
                        dve.wait_ge(sem_, (base + n[0]).count())
                    link(dve.tensor_scalar(v, var, EPS, None, ALU.add))
                    link(dve.tensor_scalar(a.bitcast(I32), v.bitcast(I32), 1, None, ALU.logical_shift_right))
                    link(dve.tensor_scalar(y.bitcast(I32), a.bitcast(I32), -1.0, MAGIC, ALU.mult, ALU.add))
                    for _ in range(3):
                        link(dve.tensor_tensor(a, y, y, ALU.mult))
                        link(dve.scalar_tensor_tensor(a, a, -0.5, v, ALU.mult, ALU.mult))
                        link(dve.scalar_tensor_tensor(y, a, 1.5, y, ALU.add, ALU.mult))

                def ln2_ops(t, first, end):
                    if t is None:
                        return
                    v, a, y = nt2[:, 0:1], nt2[:, 1:2], rs2[:, 0:1]
                    for n in range(first, end):
                        dve.wait_ge(agg2, (t + 1).count()) if n == 0 else dve.wait_ge(ln2, (t * LN2_OPS + n).count())
                        if n == 0:
                            ins = dve.tensor_scalar(v, mv2[:, 1:2], EPS, None, ALU.add)
                        elif n == 1:
                            ins = dve.tensor_scalar(a.bitcast(I32), v.bitcast(I32), 1, None, ALU.logical_shift_right)
                        elif n == 2:
                            ins = dve.tensor_scalar(y.bitcast(I32), a.bitcast(I32), -1.0, MAGIC, ALU.mult, ALU.add)
                        elif n == LN2_OPS - 1:
                            ins = dve.scalar_tensor_tensor(nb2[:, :], mv2[:, 0:1], -1.0, y, ALU.mult, ALU.mult)
                        elif n % 3 == 0:
                            ins = dve.tensor_tensor(a, y, y, ALU.mult)
                        elif n % 3 == 1:
                            ins = dve.scalar_tensor_tensor(a, a, -0.5, v, ALU.mult, ALU.mult)
                        else:
                            ins = dve.scalar_tensor_tensor(y, a, 1.5, y, ALU.add, ALU.mult)
                        ins.then_inc(ln2, 1)

                def step(k):
                    t = k.at(10)
                    if t is not None:
                        dve.wait_ge(o_done, (t + 1).count())
                        x1 = xr[:, t % 16, :]
                        dve.tensor_tensor(x1, x1, O_ps[:, :], ALU.add).then_inc(x1_done, 1)
                        dve.wait_ge(x1_done, (t + 1).count())
                        dve.bn_stats(st2[:, :], x1).then_inc(bn2, 1)
                    t8 = k.at(8)
                    if t8 is not None:
                        heads = S_ps[:, :].rearrange("p (h j) -> p h j", h=H)
                        dve.wait_ge(scores_done, (t8 + 1).count())
                        dve.tensor_reduce(top_s[:, :], heads, AX.X, ALU.max).then_inc(max_done, 1)
                    if t is not None:
                        dve.wait_ge(bn2, (t + 1).count())
                        dve.wait_ge(x2_done, t.count())
                        dve.sem_inc(passed, 1)
                        dve.bn_aggr(mv2[:, :], st2[:, :]).then_inc(agg2, 1)
                    if t8 is not None:
                        t = t8
                        dve.wait_ge(max_done, (t + 1).count())
                        dve.wait_ge(exp_done, t.count())
                        dve.tensor_tensor(below[:, :, :], heads, top_s[:, :].unsqueeze(2).to_broadcast([P, H, SKV]),
                                          ALU.subtract).then_inc(below_done, 1)
                    t10 = k.at(10)
                    ln2_ops(t10, 0, 1)
                    t = k.at(11)
                    if t is not None:
                        g, i = t // 4, t % 4
                        dve.wait_ge(x2t_hi, (t + 1).count())
                        dst = (slice(None), g % 2, slice(None), slice(i * P, (i + 1) * P))
                        dve.tensor_tensor(x2t_l[dst], TX_ps[:, :].rearrange("p (c t) -> p c t", c=KD), x2t_h[dst],
                                          ALU.subtract).then_inc(x2t_lo, 1)
                    t = k.at(9)
                    if t is not None:
                        dve.wait_ge(pt_hi, (t + 1).count())
                        dve.tensor_tensor(pt_l[:, :, :].rearrange("p a b -> p (a b)"), TP_ps[:, :],
                                          pt_h[:, :, :].rearrange("p a b -> p (a b)").bitcast(F32),
                                          ALU.subtract).then_inc(pt_lo, 1)
                    ln2_ops(t10, 1, 2)
                    if t8 is not None:
                        t = t8
                        dve.wait_ge(exp_done, (t + 1).count())
                        dve.tensor_reduce(sums[:, :], prob[:, t % 2, :, :], AX.X, ALU.add).then_inc(sum_done, 1)
                        ln2_ops(t10, 2, 3)
                        dve.wait_ge(sum_done, (t + 1).count())
                        dve.wait_ge(prob_done, t.count())
                        dve.reciprocal(rsum[:, :], sums[:, :]).then_inc(rsum_done, 1)
                    else:
                        ln2_ops(t10, 2, 3)
                    ln2_ops(t10, 3, 4)
                    for half in range(2):
                        g = k.group(5 + half)
                        if g is None:
                            continue
                        if half == 0:
                            dve.wait_ge(x_loaded[g % 4], ((g // 4) * 16 + 16).count())
                        for i in (2 * half, 2 * half + 1):
                            dve.wait_ge(agg1, (g * 4 + i - 3).count())
                            dve.bn_stats(st1[:, i, :], xr[:, 4 * (g % 4) + i, :]).then_inc(bn1, 1)
                            ln2_ops(t10, 4 + i % 2, 5 + i % 2)
                        for i in (2 * half, 2 * half + 1):
                            dve.wait_ge(bn1, (g * 4 + i + 1).count())
                            dve.sem_inc(passed, 1)
                            dve.bn_aggr(mv1[:, i, :], st1[:, i, :]).then_inc(agg1, 1)
                        if half == 1:
                            dve.wait_ge(agg1, (g * 4 + 4).count())
                            dve.wait_ge(exp_done, (g * 4 - 4).count())
                            inv_std(ln1, g * LN1_OPS, mv1[:, :, 1], nt1[:, 0, :], nt1[:, 1, :], rs1[:, g % 2, :])
                    if k.s % 4 not in (1, 2) or k.group(5) is None and k.group(6) is None:
                        ln2_ops(t10, 4, 6)
                    ln2_ops(t10, 6, 7)
                    for c in range(2):
                        g = k.group(14 + c)
                        if g is not None:
                            dve.wait_ge(th_done, (g * 2 + c + 1).count())
                            dve.scalar_tensor_tensor(th[:, :], th[:, :], 1.0, G_ps[:, :], ALU.add, ALU.mult).then_inc(g_free, 1)
                        g = k.group(16 + c)
                        if g is not None:
                            o = xr[:, 4 * (g % 4) + 2 * c, :]
                            dve.wait_ge(g_done, (g * 4 + 3 + c).count())
                            dve.scalar_tensor_tensor(o, G_ps[:, :], 0.5, o, ALU.mult, ALU.add).then_inc(g_free, 1)
                    ln2_ops(t10, 7, LN2_OPS)
                    g = k.group(15)
                    if g is not None:
                        n = [0]

                        def link(ins):
                            n[0] += 1
                            ins.then_inc(route_a, 1)

                        def sync():
                            dve.wait_ge(route_a, (g * ROUTE_A + n[0]).count())
                        dve.wait_ge(lexp_done, (g + 1).count())
                        link(dve.tensor_scalar(lexp[:, :, :], lexp[:, :, :], 1.0, None, ALU.add))
                        sync()
                        link(dve.reciprocal(score[:, :, :], lexp[:, :, :]))
                        sync()
                        link(dve.tensor_tensor(biased[:, :, :], score[:, :, :],
                                               bias_sb[:, :].unsqueeze(1).to_broadcast([P, 4, E]), ALU.add))
                        dve.wait_ge(route_a, (g * ROUTE_A + n[0]).count())
                        dve.sem_inc(passed, 1)
                        for i in range(4):
                            link(dve.max(best[:, i, :], biased[:, i, :]))
                        dve.wait_ge(route_a, (g * ROUTE_A + n[0]).count())
                        dve.sem_inc(passed, 1)
                        for i in range(4):
                            link(dve.max_index(best_at[:, i, :], best[:, i, :], biased[:, i, :]))
                        sync()
                        link(dve.tensor_copy(best_f[:, :, :], best_at[:, :, 0:TOP]))
                        sync()
                        dve.wait_ge(route_b, (g * ROUTE_B).count())
                        link(dve.tensor_tensor(
                            pick[:, :, :], iota_e[:, :].unsqueeze(1).to_broadcast([P, 4 * TOP, E]),
                            best_f[:, :, :].rearrange("p i k -> p (i k)").unsqueeze(2).to_broadcast([P, 4 * TOP, E]),
                            ALU.is_equal))
                        sync()
                        dve.wait_ge(rank_done, g.count())
                        if not (isinstance(g.value(), int) and g.value() == 0):
                            dve.tensor_reduce(gsum[:, :], member[:, :, :].rearrange("p i e -> p e i"), AX.X, ALU.add).then_inc(joined, 1)
                            dve.wait_ge(joined, (g * 2 - 1).count())
                            dve.tensor_tensor(before[:, :], before[:, :], gsum[:, :], ALU.add).then_inc(joined, 1)
                            dve.wait_ge(joined, (g * 2).count())
                        with nc.allow_low_precision("counts of zero and one are exact"):
                            link(dve.tensor_reduce(member[:, :, :], pick[:, :, :].rearrange("p (i k) e -> p i e k", k=TOP),
                                                   AX.X, ALU.add))
                        assert n[0] == ROUTE_A, n
                    g = k.group(16)
                    if g is not None:
                        n = [0]

                        def link(ins):
                            n[0] += 1
                            ins.then_inc(route_b, 1)
                            dve.wait_ge(route_b, (g * ROUTE_B + n[0]).count())
                        dve.wait_ge(route_a, (g * ROUTE_A + ROUTE_A).count())
                        link(dve.tensor_tensor(wm[:, :, :], member[:, :, :], score[:, :, :], ALU.mult))
                        link(dve.tensor_reduce(wsum[:, :], wm[:, :, :], AX.X, ALU.add))
                        link(dve.tensor_scalar(wsum[:, :], wsum[:, :], 1e-12, None, ALU.max))
                        link(dve.reciprocal(wr[:, :], wsum[:, :]))
                        link(dve.tensor_scalar(wr[:, :], wr[:, :], 0.5, None, ALU.mult))
                        dve.wait_ge(w_stored[g % 2], ((g // 2) * 16).count())
                        dve.tensor_tensor(wfull[:, g % 2], wm[:, :, :], wr[:, :].unsqueeze(2).to_broadcast([P, 4, E]),
                                          ALU.mult).then_inc(w_ready, 1)
                    g = k.group(17)
                    if g is not None:
                        n = [5]

                        def link(ins):
                            n[0] += 1
                            ins.then_inc(route_b, 1)
                            dve.wait_ge(route_b, (g * ROUTE_B + n[0]).count())
                        dve.wait_ge(rank_done, (g + 1).count())
                        link(dve.tensor_tensor(pick[:, :, :].rearrange("p (i k) e -> p i k e", k=TOP),
                                               pick[:, :, :].rearrange("p (i k) e -> p i k e", k=TOP),
                                               rank_ps.unsqueeze(2).to_broadcast([P, 4, TOP, E]), ALU.mult))
                        link(dve.tensor_reduce(pos_k[:, :], pick[:, :, :], AX.X, ALU.add))
                        link(dve.tensor_scalar(over[:, :], pos_k[:, :], float(CAP), SKIP, ALU.is_ge, ALU.mult))
                        link(dve.scalar_tensor_tensor(slot_f[:, :], best_f[:, :, :].rearrange("p i k -> p (i k)"), float(CAP),
                                                      pos_k[:, :], ALU.mult, ALU.add))
                        dve.wait_ge(scattered[(g - 2) % 4], (((g - 2) // 4) * 256 + 256).count())
                        dve.tensor_tensor(slot[:, g % 2, :], slot_f[:, :], over[:, :], ALU.add).then_inc(slots_ready, 1)
                        assert n[0] == ROUTE_B, n
                    for c in range(2):
                        g = k.group(14 + c)
                        if g is not None:
                            dve.wait_ge(u_done, (g * 4 + c + 1).count())
                            dve.wait_ge(g_free, (g * 4 + c + 1).count())
                            dve.wait_ge(ht_lo, (g * 2 + c).count())
                            dve.tensor_tensor(hid[:, :], th[:, :], U_ps[:, :], ALU.mult).then_inc(u_free, 1)
                        g = k.group(16 + c)
                        if g is not None:
                            o = xr[:, 4 * (g % 4) + 2 * c + 1, :]
                            dve.wait_ge(u_done, (g * 4 + 3 + c).count())
                            dve.scalar_tensor_tensor(o, U_ps[:, :], 0.5, o, ALU.mult, ALU.add).then_inc(u_free, 1)

                steps(dve, step)


EBODY = 4
ELAST = 4
CHUNKS = CAP // P


class ExpertStep:

    def __init__(self, it, s):
        self.it, self.s = it, s

    def at(self, lag):
        n = Index(self.it, EBODY, self.s - lag)
        if isinstance(self.it, int) and not 0 <= n.value() < E:
            return None
        return n


def expert_steps(eng, step):
    for n in range(EBODY):
        step(ExpertStep(0, n))
    with eng.Fori(1, E // EBODY) as it:
        for s in range(EBODY):
            step(ExpertStep(it, s))
    for n in range(E, E + ELAST):
        step(ExpertStep(n // EBODY, n % EBODY))


def experts(nc, w1, w3, w2, out, x2aug, table):
    stack = ExitStack()
    with stack:
        def sb(name, shape, dt):
            return stack.enter_context(nc.sbuf_tensor(name, shape, dt))

        def pb(name):
            return stack.enter_context(nc.psum_tensor(name, [P, 512], F32))

        def sem(name):
            return stack.enter_context(nc.semaphore(name))

        ident_f = sb("ident_f", [P, P], F32)
        ident_r = sb("ident_r", [P, P], F32R)
        idx_g = sb("idx_g", [P, 4, CHUNKS], I32)
        idx_s = sb("idx_s", [P, 4, CHUNKS], I32)
        rows = sb("rows", [P, 4, CHUNKS, ROW], F32R)
        up_w = sb("up_w", [P, 4, KD, 2 * I], BF16)
        down_raw = sb("down_raw", [P, 4, KI, D], BF16)
        down_w = sb("down_w", [P, 2, KI, D], F32R)
        xe_h = sb("xe_h", [P, 2, KD, CAP], F16)
        xe_l = sb("xe_l", [P, 2, KD, CAP], F16)
        the = sb("the", [P, 2, CAP], F32)
        gte = sb("gte", [P, 2, CAP], F32)
        hie = sb("hie", [P, 2, CAP], F32)
        he_h = sb("he_h", [P, 2, KI, CAP], F32R)
        he_l = sb("he_l", [P, 2, KI, CAP], F32R)
        ye = sb("ye", [P, 2, CHUNKS, D], F32)

        TE_ps = [pb(f"TE_ps{n}") for n in range(2)]
        GE_ps = [pb(f"GE_ps{n}") for n in range(KI)]
        UE_ps = [pb(f"UE_ps{n}") for n in range(KI)]
        YE_ps = [pb(f"YE_ps{n}") for n in range(2)]

        idx_g_loaded = [sem(f"idx_g_loaded{n}") for n in range(4)]
        idx_s_loaded = [sem(f"idx_s_loaded{n}") for n in range(4)]
        up_loaded = [sem(f"up_loaded{n}") for n in range(4)]
        down_loaded = [sem(f"down_loaded{n}") for n in range(4)]
        gathered = [sem(f"gathered{n}") for n in range(4)]
        added = sem("added")
        passed = sem("passed")
        ident_p, ident_ready = sem("ident_p"), sem("ident_ready")
        t_done, t_hi, t_lo = sem("t_done"), sem("t_hi"), sem("t_lo")
        ge_done, ue_done, y_done = sem("ge_done"), sem("ue_done"), sem("y_done")
        down_ready, the_done, he_hi = sem("down_ready"), sem("the_done"), sem("he_hi")
        gte_done, hie_done, he_lo, y_read = sem("gte_done"), sem("hie_done"), sem("he_lo"), sem("y_read")

        up_src = [w.rearrange("e (c p) i -> e p c i", p=P) for w in (w1, w3)]
        down_src = w2.rearrange("e (c p) d -> e p c d", p=P)
        table_src = table.rearrange("(e p c) o -> e p (c o)", e=E, p=P)

        with nc.Block() as block:
            @block.sync
            def _(sp):
                def step(k):
                    e = k.at(0)
                    if e is not None:
                        r = e % 4
                        sp.wait_ge(gathered[r], ((e // 4) * 64).count())
                        sp.dma_start(idx_g[:, r, :], table_src[e.value()]).then_inc(idx_g_loaded[r], 16)
                        sp.wait_ge(added, (e * 64 - 192).count())
                        sp.dma_start(idx_s[:, r, :], table_src[e.value()]).then_inc(idx_s_loaded[r], 16)
                        sp.wait_ge(ue_done, (e * 2 - 6).count())
                        for n in range(2):
                            sp.dma_start(up_w[:, r, :, n * I:(n + 1) * I], up_src[n][e.value()]).then_inc(up_loaded[r], 16)
                        sp.wait_ge(down_ready, (e - 3).count())
                        sp.dma_start(down_raw[:, r, :, :], down_src[e.value()]).then_inc(down_loaded[r], 16)
                expert_steps(sp, step)

            @block.gpsimd
            def _(pool):
                pool.memset(ident_f[:, :], 0.0).then_inc(ident_p, 1)
                pool.wait_ge(ident_p, 1)
                pool.affine_select(out=ident_f[:, :], in_=ident_f[:, :], compare_op=ALU.not_equal, fill=1.0,
                                   base=0, pattern=[[-1, P]], channel_multiplier=1).then_inc(ident_p, 1)

                def step(k):
                    e = k.at(0)
                    if e is not None:
                        r = e % 4
                        pool.wait_ge(idx_g_loaded[r], ((e // 4) * 16 + 16).count())
                        pool.wait_ge(y_read, (e * CHUNKS - 12).count())
                        pool.sem_inc(passed, 1)
                        for c in range(CHUNKS):
                            pool.indirect_dma_start(
                                rows[:, r, c, :].bitcast(F32), None, x2aug,
                                bass.IndirectOffsetOnAxis(ap=idx_g[:, r, c:c + 1], axis=0),
                                bounds_check=TOKENS + PAD - 1, oob_is_err=False).then_inc(gathered[r], 16)
                    e = k.at(4)
                    if e is not None:
                        r = e % 4
                        pool.wait_ge(idx_s_loaded[r], ((e // 4) * 16 + 16).count())
                        pool.wait_ge(y_read, (e * CHUNKS + CHUNKS).count())
                        pool.wait_ge(added, (e * 64).count())
                        pool.sem_inc(passed, 1)
                        for c in range(CHUNKS):
                            pool.indirect_dma_start(
                                out, bass.IndirectOffsetOnAxis(ap=idx_s[:, r, c:c + 1], axis=0),
                                ye[:, e % 2, c, :], None, bounds_check=TOKENS + PAD - 1, oob_is_err=True,
                                compute_op=ALU.add).then_inc(added, 16)
                expert_steps(pool, step)
                pool.wait_ge(added, E * 64)

            @block.tensor
            def _(pe):
                def up_half(bank, e, w0, c):
                    n = 0
                    for kc in range(KD):
                        for part in (xe_h, xe_l):
                            last = pe.matmul(bank[:, :], up_w[:, e % 4, kc, w0 + c * P:w0 + (c + 1) * P],
                                             part[:, e % 2, kc, :], start=(n == 0), stop=(n == 2 * KD - 1))
                            n += 1
                    return last

                def down_chunk(e, i):
                    pe.wait_ge(y_read, (e * CHUNKS + i - 1).count())
                    n = 0
                    for c in range(KI):
                        for part in (he_h, he_l):
                            last = pe.matmul(YE_ps[i % 2][:, :], part[:, e % 2, c, i * P:(i + 1) * P],
                                             down_w[:, e % 2, c, :], start=(n == 0), stop=(n == 2 * KI - 1))
                            n += 1
                    last.then_inc(y_done, 1)

                def step(k):
                    for c in range(KI):
                        e = k.at(2)
                        if e is not None:
                            if c == 0:
                                pe.wait_ge(up_loaded[e % 4], ((e // 4) * 32 + 32).count())
                                pe.wait_ge(t_hi, (e * CHUNKS + CHUNKS).count())
                                pe.wait_ge(t_lo, (e * CHUNKS + CHUNKS).count())
                            pe.wait_ge(gte_done, (e * 2 + c - 1).count())
                            up_half(GE_ps[c], e, 0, c).then_inc(ge_done, 1)
                            pe.wait_ge(hie_done, (e * 2 + c - 1).count())
                            up_half(UE_ps[c], e, I, c).then_inc(ue_done, 1)
                        e = k.at(1)
                        if e is not None:
                            pe.wait_ge(gathered[e % 4], ((e // 4) * 64 + 64).count())
                            for i in (2 * c, 2 * c + 1):
                                pe.wait_ge(t_hi, (e * CHUNKS + i - 1).count())
                                pe.wait_ge(t_lo, (e * CHUNKS + i - 1).count())
                                for kc in range(KD):
                                    last = pe.transpose(TE_ps[i % 2][:, kc * P:(kc + 1) * P].bitcast(F32R),
                                                        rows[:, e % 4, i, kc * P:(kc + 1) * P], ident_r[:, :])
                                last.then_inc(t_done, 1)
                        e = k.at(3)
                        if e is not None:
                            if c == 0:
                                pe.wait_ge(he_hi, (e * 2 + 2).count())
                                pe.wait_ge(he_lo, (e * 2 + 2).count())
                                pe.wait_ge(down_ready, (e + 1).count())
                            down_chunk(e, 2 * c)
                            down_chunk(e, 2 * c + 1)
                pe.wait_ge(ident_ready, 1)
                expert_steps(pe, step)

            @block.scalar
            def _(act):
                act.wait_ge(ident_p, 2)
                act.activation(ident_r[:, :], ident_f[:, :], ACT.Copy).then_inc(ident_ready, 1)

                def step(k):
                    for c in range(KI):
                        e = k.at(2)
                        if e is not None:
                            act.wait_ge(ge_done, (e * 2 + c + 1).count())
                            act.wait_ge(gte_done, (e * 2 + c - 1).count())
                            act.activation(the[:, c, :], GE_ps[c][:, :], ACT.Tanh, scale=0.5).then_inc(the_done, 1)
                            if c == 0:
                                act.wait_ge(down_loaded[e % 4], ((e // 4) * 16 + 16).count())
                                act.wait_ge(y_done, (e * CHUNKS - 4).count())
                                act.activation(down_w[:, e % 2, :, :], down_raw[:, e % 4, :, :], ACT.Copy).then_inc(down_ready, 1)
                            act.wait_ge(hie_done, (e * 2 + c + 1).count())
                            act.wait_ge(y_done, (e * CHUNKS - 4).count())
                            act.activation(he_h[:, e % 2, c, :], hie[:, c, :], ACT.Copy).then_inc(he_hi, 1)
                        e = k.at(1)
                        for i in (2 * c, 2 * c + 1):
                            if e is None:
                                continue
                            act.wait_ge(t_done, (e * CHUNKS + i + 1).count())
                            act.wait_ge(ue_done, (e * 2 - 2).count())
                            act.activation(xe_h[:, e % 2, :, i * P:(i + 1) * P],
                                           TE_ps[i % 2][:, :].rearrange("p (c t) -> p c t", c=KD), ACT.Copy).then_inc(t_hi, 1)
                expert_steps(act, step)

            @block.vector
            def _(dve):
                def weighted(k, i):
                    e = k.at(3)
                    if e is None:
                        return
                    if i == 0:
                        dve.wait_ge(added, (e * 64 - 64).count())
                    dve.wait_ge(y_done, (e * CHUNKS + i + 1).count())
                    w = rows[:, e % 4, i, :].bitcast(F32)[:, bass.ds(e.value() + D, 1)]
                    dve.tensor_scalar(ye[:, e % 2, i, :], YE_ps[i % 2][:, :], w, None, ALU.mult).then_inc(y_read, 1)

                def step(k):
                    for c in range(KI):
                        e = k.at(2)
                        if e is not None:
                            dve.wait_ge(the_done, (e * 2 + c + 1).count())
                            dve.wait_ge(hie_done, (e * 2 + c - 1).count())
                            dve.scalar_tensor_tensor(gte[:, c, :], the[:, c, :], 1.0, GE_ps[c][:, :], ALU.add, ALU.mult).then_inc(gte_done, 1)
                            dve.wait_ge(ue_done, (e * 2 + c + 1).count())
                            dve.wait_ge(gte_done, (e * 2 + c + 1).count())
                            dve.wait_ge(he_lo, (e * 2 + c - 1).count())
                            dve.tensor_tensor(hie[:, c, :], gte[:, c, :], UE_ps[c][:, :], ALU.mult).then_inc(hie_done, 1)
                            dve.wait_ge(he_hi, (e * 2 + c + 1).count())
                            dve.tensor_tensor(he_l[:, e % 2, c, :], hie[:, c, :], he_h[:, e % 2, c, :].bitcast(F32),
                                              ALU.subtract).then_inc(he_lo, 1)
                        e = k.at(1)
                        for i in (2 * c, 2 * c + 1):
                            if e is None:
                                continue
                            dve.wait_ge(t_hi, (e * CHUNKS + i + 1).count())
                            dst = (slice(None), e % 2, slice(None), slice(i * P, (i + 1) * P))
                            dve.tensor_tensor(xe_l[dst], TE_ps[i % 2][:, :].rearrange("p (c t) -> p c t", c=KD), xe_h[dst],
                                              ALU.subtract).then_inc(t_lo, 1)
                        weighted(k, 2 * c)
                        weighted(k, 2 * c + 1)
                expert_steps(dve, step)


def kernel(**inputs):
    import concourse.bacc as bacc
    import numpy as np
    from concourse.bass_utils import run_bass_kernel_spmd

    def plain(name):
        return np.asarray(inputs[name])

    x = plain("x").reshape(TOKENS, D)
    arrays = {
        "x": x,
        "xT": x.reshape(TILES, P, KD, P).transpose(0, 3, 2, 1),
        "ctxT": plain("ctx_768").transpose(0, 2, 1),
        "wqT": plain("L0_xattn_Wq").T,
        "wk": plain("L0_xattn_Wk"),
        "wv": plain("L0_xattn_Wv"),
        "wo": plain("L0_xattn_Wo"),
        "bo": plain("L0_xattn_bo"),
        "gateT": plain("L0_ffn_gate_w").T,
        "bias": np.broadcast_to(plain("L0_ffn_bias"), (P, E)),
        "w1": plain("L0_ffn_W1"),
        "w3": plain("L0_ffn_W3"),
        "w2": plain("L0_ffn_W2"),
        "sw1T": plain("L0_ffn_sw1").T,
        "sw3T": plain("L0_ffn_sw3").T,
        "sw2T": plain("L0_ffn_sw2").T,
    }
    arrays = {f"in_{n}": np.ascontiguousarray(a) for n, a in arrays.items()}
    nc = bacc.Bacc("TRN2", target_bir_lowering=False, num_devices=1)
    args = [nc.dram_tensor(n, a.shape, mybir.dt.from_np(a.dtype), kind="ExternalInput").ap() for n, a in arrays.items()]
    out = nc.dram_tensor("out", (TOKENS + PAD, D), F32, kind="ExternalOutput").ap()
    build(nc, *args, out)
    r = run_bass_kernel_spmd(nc, [arrays], core_ids=[0])
    return r.results[0]["out"][0:TOKENS].reshape(B, S, D)
```
